# Optimizing a Trainium2 kernel written in Bass

```python
import numpy as np
import jax
import jax.numpy as jnp

def _softmax(x, axis=-1):
    return jax.nn.softmax(x, axis=axis)
def _gelu(x):
    return jax.nn.gelu(x, approximate=True)
def _silu(x):
    return jax.nn.silu(x)
def _sigmoid(x):
    return jax.nn.sigmoid(x)
def _layernorm(x, axis=-1, eps=1e-5):
    m = jnp.mean(x, axis=axis, keepdims=True)
    v = jnp.var(x, axis=axis, keepdims=True)
    return (x - m) / jnp.sqrt(v + eps)
def _scatter_add(tgt, idx, src, axis=0):
    return tgt.at[idx].add(src)
def _segment_sum(src, seg, n):
    return jax.ops.segment_sum(src, seg, n)

kernel_name = 'mk_conv_preact_d1_conv_nchw128_225164'

def setup_inputs(seed: int = 0):
    np.random.seed(seed)
    _w = jnp.asarray
    def _rec_inputs():
        import jax
        import jax.numpy as jnp
        _gk = jax.random.key(seed)
        x = -0.0002091 + 1 * jax.random.normal(jax.random.fold_in(_gk, 1), (64, 128, 56, 56), jnp.float32)
        return x
    x = _rec_inputs()
    def _L0_conv_setup():
        import jax, jax.numpy as jnp
        import numpy as np
        BN_EPS = 1e-05

        def binary_activation(x):
            out_fwd = jnp.sign(x)
            m1 = (x < -1.0).astype(x.dtype)
            m2 = (x < 0.0).astype(x.dtype)
            m3 = (x < 1.0).astype(x.dtype)
            out1 = -1.0 * m1 + (x * x + 2.0 * x) * (1.0 - m1)
            out2 = out1 * m2 + (-x * x + 2.0 * x) * (1.0 - m2)
            out3 = out2 * m3 + 1.0 * (1.0 - m3)
            return jax.lax.stop_gradient(out_fwd - out3) + out3

        def binary_conv3x3(x, w, stride=1):
            scale = jax.lax.stop_gradient(jnp.mean(jnp.abs(w), axis=(1, 2, 3), keepdims=True))
            bw_no_grad = jax.lax.stop_gradient(scale * jnp.sign(w))
            cw = jnp.clip(w, -1.0, 1.0)
            bw = bw_no_grad - jax.lax.stop_gradient(cw) + cw
            return jax.lax.conv_general_dilated(x, bw, window_strides=(stride, stride), padding=[(1, 1), (1, 1)], dimension_numbers=('NCHW', 'OIHW', 'NCHW'))

        def batchnorm_inference(y, gamma, beta, mean, var):
            inv = gamma * jax.lax.rsqrt(var + BN_EPS)
            return y * inv[None, :, None, None] + (beta - mean * inv)[None, :, None, None]
        key = jax.random.key(seed)
        k1, k2, k3 = jax.random.split(key, 3)
        N, Cin, Cout, H, W = (64, 128, 128, 56, 56)
        x = jax.random.normal(k1, (N, Cin, H, W), dtype=jnp.float32)
        weight = jax.random.normal(k2, (Cout, Cin, 3, 3), dtype=jnp.float32) * 0.1
        gamma = jnp.ones((Cout,), dtype=jnp.float32)
        beta = jnp.zeros((Cout,), dtype=jnp.float32)
        bn_mean = jnp.zeros((Cout,), dtype=jnp.float32)
        bn_var = jax.random.uniform(k3, (Cout,), dtype=jnp.float32)
        return {'x': x, 'weight': weight, 'gamma': gamma, 'beta': beta, 'bn_mean': bn_mean, 'bn_var': bn_var}
    _L0_conv_all = _L0_conv_setup()
    _L0_conv_in = {k: v for k, v in _L0_conv_all.items() if k in ('weight', 'gamma', 'beta', 'bn_mean', 'bn_var', )}
    del _L0_conv_all

    return {
        "x": x,
        "L0_conv_weight": _L0_conv_in["weight"],
        "L0_conv_gamma": _L0_conv_in["gamma"],
        "L0_conv_beta": _L0_conv_in["beta"],
        "L0_conv_bn_mean": _L0_conv_in["bn_mean"],
        "L0_conv_bn_var": _L0_conv_in["bn_var"],
    }

def reference(x, L0_conv_weight, L0_conv_gamma, L0_conv_beta, L0_conv_bn_mean, L0_conv_bn_var):
    import jax
    import jax.numpy as jnp
    def _L0_conv_ref(x, weight, gamma, beta, bn_mean, bn_var):
        import jax, jax.numpy as jnp
        import numpy as np
        BN_EPS = 1e-05

        def binary_activation(x):
            out_fwd = jnp.sign(x)
            m1 = (x < -1.0).astype(x.dtype)
            m2 = (x < 0.0).astype(x.dtype)
            m3 = (x < 1.0).astype(x.dtype)
            out1 = -1.0 * m1 + (x * x + 2.0 * x) * (1.0 - m1)
            out2 = out1 * m2 + (-x * x + 2.0 * x) * (1.0 - m2)
            out3 = out2 * m3 + 1.0 * (1.0 - m3)
            return jax.lax.stop_gradient(out_fwd - out3) + out3

        def binary_conv3x3(x, w, stride=1):
            scale = jax.lax.stop_gradient(jnp.mean(jnp.abs(w), axis=(1, 2, 3), keepdims=True))
            bw_no_grad = jax.lax.stop_gradient(scale * jnp.sign(w))
            cw = jnp.clip(w, -1.0, 1.0)
            bw = bw_no_grad - jax.lax.stop_gradient(cw) + cw
            return jax.lax.conv_general_dilated(x, bw, window_strides=(stride, stride), padding=[(1, 1), (1, 1)], dimension_numbers=('NCHW', 'OIHW', 'NCHW'))

        def batchnorm_inference(y, gamma, beta, mean, var):
            inv = gamma * jax.lax.rsqrt(var + BN_EPS)
            return y * inv[None, :, None, None] + (beta - mean * inv)[None, :, None, None]
        residual = x
        out = binary_activation(x)
        out = binary_conv3x3(out, weight, stride=1)
        out = batchnorm_inference(out, gamma, beta, bn_mean, bn_var)
        return out + residual

    def _gn(v, G=32, eps=1e-5):
        B_, C_, H_, W_ = v.shape
        g = v.reshape(B_, G, C_ // G, H_, W_)
        m = jnp.mean(g, axis=(2, 3, 4), keepdims=True)
        s = jnp.var(g, axis=(2, 3, 4), keepdims=True)
        return ((g - m) / jnp.sqrt(s + eps)).reshape(v.shape)

    def _ln_c(v, eps=1e-6):
        m = jnp.mean(v, axis=1, keepdims=True)
        s = jnp.var(v, axis=1, keepdims=True)
        return (v - m) / jnp.sqrt(s + eps)

    def _ln_t(v, eps=1e-5):
        m = jnp.mean(v, axis=-1, keepdims=True)
        s = jnp.var(v, axis=-1, keepdims=True)
        return (v - m) / jnp.sqrt(s + eps)

    def _to_tokens(v):
        B_, C_, H_, W_ = v.shape
        return v.reshape(B_, C_, H_ * W_).transpose(0, 2, 1)
    def _from_tokens(t, like):
        B_, C_, H_, W_ = like.shape
        return t.transpose(0, 2, 1).reshape(B_, C_, H_, W_)

    x = x + _L0_conv_ref(_gn(x), L0_conv_weight, L0_conv_gamma, L0_conv_beta, L0_conv_bn_mean, L0_conv_bn_var)
    return x


_drawn_inputs = setup_inputs


def setup_inputs(seed=0):
    import zlib

    import numpy as np

    out = dict(_drawn_inputs(seed))
    spreads = {'L0_conv_gamma': (1.0, 0.2), 'L0_conv_beta': (0.0, 0.513), 'L0_conv_bn_mean': (0.0, 0.328)}
    factors = {}
    for name, (base, spread) in spreads.items():
        noise = np.random.default_rng([zlib.crc32(name.encode()), seed]).standard_normal(out[name].shape)
        drawn = base * np.exp(spread * noise) if base else spread * noise
        out[name] = jnp.asarray(drawn.astype(out[name].dtype))
    for name, factor in factors.items():
        out[name] = (out[name] * factor).astype(out[name].dtype)
    return out
```

```python
from contextlib import ExitStack

import concourse.bass as bass
from concourse import mybir

F32 = mybir.dt.float32
BF16 = mybir.dt.bfloat16
ALU = mybir.AluOpType
ACT = mybir.ActivationFunctionType
AX_X = mybir.AxisListType.X

GN_EPS = 1e-5
BN_EPS = 1e-5


def gn_binary_conv_kernel(nc: bass.Bass, x: bass.AP, weight: bass.AP, gamma: bass.AP, beta: bass.AP,
                          bn_mean: bass.AP, bn_var: bass.AP, out: bass.AP):
    N, C, H, W = x.shape
    O, _, KH, KW = weight.shape
    assert C == 128 and O == 128 and KH == 3 and KW == 3
    GROUPS = 32
    CG = C // GROUPS
    HW = H * W
    TAPS = KH * KW
    ROWS = 8
    CHUNK = ROWS * W
    CHUNKS = H // ROWS
    WP = W + 2
    U = 4
    SG = 2
    STEPS = N // U
    STATS_AFTER = 4

    x_v = x.rearrange("n c h w -> n c (h w)")
    out_v = out.rearrange("n c h w -> n c (h w)")
    w_v = weight.rearrange("o c kh kw -> o (c kh kw)")

    taps = sorted(((ky, kx) for ky in range(KH) for kx in range(KW)), key=lambda t: (t[0] != 1, t))

    with ExitStack() as ctx:
        def sb(name, shape, dt=F32):
            return ctx.enter_context(nc.sbuf_tensor(name, shape, dt))

        def psum(name, shape, dt=F32):
            return ctx.enter_context(nc.psum_tensor(name, shape, dt))

        def sem(name):
            return ctx.enter_context(nc.semaphore(name))

        xt = [sb(f"xt{i}", [C, HW]) for i in range(U)]
        sg = [sb(f"sg{i}", [C, H, WP], BF16) for i in range(SG)]
        tuples = [sb(f"tuples{i}", [C, CHUNKS, 6]) for i in range(SG)]
        chan = [sb(f"chan{i}", [C, 3]) for i in range(SG)]
        spread = [sb(f"spread{i}", [C, CG, 3]) for i in range(SG)]
        group = [sb(f"group{i}", [C, 2]) for i in range(SG)]
        gtuples = sb("gtuples", [C, CG * 3])
        negm = [sb(f"negm{i}", [C, 1]) for i in range(SG)]
        vare = [sb(f"vare{i}", [C, 1]) for i in range(SG)]
        rstd = [sb(f"rstd{i}", [C, 1]) for i in range(SG)]
        xscale = [sb(f"xscale{i}", [C, 1]) for i in range(SG)]
        negmr = [sb(f"negmr{i}", [C, 1]) for i in range(SG)]
        xbias = [sb(f"xbias{i}", [C, 1]) for i in range(SG)]

        ident = sb("ident", [C, C], BF16)
        same = sb("same", [C, GROUPS, CG])
        place = sb("place", [C, CG])
        halfneg = sb("halfneg", [C, 1])
        gneps = sb("gneps", [C, 1])
        one = sb("one", [C, 1])
        wraw = sb("wraw", [O, C * TAPS])
        wabs = sb("wabs", [O, C * TAPS])
        wsign = sb("wsign", [O, C, TAPS], BF16)
        wT = sb("wT", [C, TAPS, O], BF16)
        wsum = sb("wsum", [O, 1])
        bn = sb("bn", [O, 4])
        bnvare = sb("bnvare", [O, 1])
        bnr = sb("bnr", [O, 1])
        inv = sb("inv", [O, 1])
        minv = sb("minv", [O, 1])
        obias = sb("obias", [O, 1])
        wmean = sb("wmean", [O, 1])
        oscale = sb("oscale", [O, 1])

        conv = [psum(f"conv{c}", [O, 512]) for c in range(CHUNKS)]
        small = psum("small", [C, 512])

        x_loaded = [sem(f"x_loaded{i}") for i in range(U)]
        stored = [sem(f"stored{i}") for i in range(U)]
        w_loaded = sem("w_loaded")
        bn_loaded = sem("bn_loaded")
        pool_step = sem("pool_step")
        ident_ready = sem("ident_ready")
        same_ready = sem("same_ready")
        bn_ready = sem("bn_ready")
        w_signed = sem("w_signed")
        w_turned = sem("w_turned")
        w_ready = sem("w_ready")
        const_ready = sem("const_ready")
        oscale_ready = sem("oscale_ready")
        dve_step = sem("dve_step")
        chan_ready = sem("chan_ready")
        spread_ready = sem("spread_ready")
        summed = sem("summed")
        group_ready = sem("group_ready")
        negm_ready = sem("negm_ready")
        vare_ready = sem("vare_ready")
        rstd_ready = sem("rstd_ready")
        negmr_ready = sem("negmr_ready")
        affine_ready = sem("affine_ready")
        signed = sem("signed")
        scaled = sem("scaled")
        conv_done = sem("conv_done")
        chunk_done = sem("chunk_done")

        block = ctx.enter_context(nc.Block())

        @block.sync
        def _(sp):
            sp.dma_start(wraw[:, :], w_v).then_inc(w_loaded, 16)
            for k, vec in enumerate((gamma, beta, bn_mean, bn_var)):
                sp.dma_start(bn[:, k:k + 1], vec.rearrange("(c a) -> c a", a=1)).then_inc(bn_loaded, 16)
            for u in range(U - 1):
                sp.dma_start(xt[u][:, :], x_v[u]).then_inc(x_loaded[u], 16)

            def store(s, u):
                sp.wait_ge(chunk_done, (s * U + u + 1) * CHUNKS)
                sp.dma_start(out_v[s * U + u], xt[u][:, :]).then_inc(stored[u], 16)

            store(0, 0)
            sp.dma_start(xt[U - 1][:, :], x_v[U - 1]).then_inc(x_loaded[U - 1], 16)
            for u in range(1, U):
                store(0, u)
                sp.wait_ge(stored[u - 1], 16)
                sp.dma_start(xt[u - 1][:, :], x_v[U + u - 1]).then_inc(x_loaded[u - 1], 16)
            with sp.Fori(1, STEPS - 1) as s:
                store(s, 0)
                sp.wait_ge(stored[U - 1], s * 16)
                sp.dma_start(xt[U - 1][:, :], x_v[s * U + U - 1]).then_inc(x_loaded[U - 1], 16)
                for u in range(1, U):
                    store(s, u)
                    sp.wait_ge(stored[u - 1], (s + 1) * 16)
                    sp.dma_start(xt[u - 1][:, :], x_v[s * U + U + u - 1]).then_inc(x_loaded[u - 1], 16)
            s = STEPS - 1
            store(s, 0)
            sp.wait_ge(stored[U - 1], s * 16)
            sp.dma_start(xt[U - 1][:, :], x_v[N - 1]).then_inc(x_loaded[U - 1], 16)
            for u in range(1, U):
                store(s, u)
            for u in range(U):
                sp.wait_ge(stored[u], STEPS * 16)

        @block.gpsimd
        def _(pool):
            count = [0]

            def chain(ins):
                count[0] += 1
                ins.then_inc(pool_step, 1)
                pool.wait_ge(pool_step, count[0])

            chain(pool.memset(ident[:, :], 0.0))
            pool.affine_select(out=ident[:, :], in_=ident[:, :], compare_op=ALU.not_equal, fill=1.0, base=0,
                               pattern=[[-1, C]], channel_multiplier=1).then_inc(ident_ready, 1)
            chain(pool.memset(same[:, :, :], 1.0))
            chain(pool.affine_select(out=same[:, :, :], in_=same[:, :, :], compare_op=ALU.is_ge, fill=0.0, base=0,
                                     pattern=[[-CG, GROUPS], [0, CG]], channel_multiplier=1))
            pool.affine_select(out=same[:, :, :], in_=same[:, :, :], compare_op=ALU.is_ge, fill=0.0, base=CG - 1,
                               pattern=[[CG, GROUPS], [0, CG]], channel_multiplier=-1).then_inc(same_ready, 1)
            chain(pool.memset(halfneg[:, :], -0.5))
            chain(pool.memset(gneps[:, :], GN_EPS))
            chain(pool.memset(one[:, :], 1.0))
            pool.wait_ge(bn_loaded, 64)
            chain(pool.tensor_scalar(bnvare[:, :], bn[:, 3:4], BN_EPS, None, ALU.add))
            chain(pool.tensor_tensor(bnr[:, :], bnvare[:, :], halfneg[:, :], ALU.pow))
            chain(pool.tensor_tensor(inv[:, :], bnr[:, :], bn[:, 0:1], ALU.mult))
            chain(pool.tensor_tensor(minv[:, :], inv[:, :], bn[:, 2:3], ALU.mult))
            pool.tensor_tensor(obias[:, :], bn[:, 1:2], minv[:, :], ALU.subtract).then_inc(bn_ready, 1)
            pool.wait_ge(bn_ready, 1)

            def image(s, u):
                n, b = s * U + u, u % SG
                pool.wait_ge(group_ready, n + 1)
                pool.tensor_tensor(vare[b][:, :], group[b][:, 1:2], gneps[:, :], ALU.add).then_inc(vare_ready, 1)
                pool.wait_ge(vare_ready, n + 1)
                pool.tensor_tensor(rstd[b][:, :], vare[b][:, :], halfneg[:, :], ALU.pow).then_inc(rstd_ready, 1)
                pool.wait_ge(rstd_ready, n + 1)
                pool.wait_ge(negm_ready, n + 1)
                pool.tensor_tensor(negmr[b][:, :], negm[b][:, :], rstd[b][:, :], ALU.mult).then_inc(negmr_ready, 1)
                if u >= SG or not isinstance(s, int):
                    pool.wait_ge(scaled, n - SG + 1)
                pool.tensor_tensor(xscale[b][:, :], rstd[b][:, :], one[:, :], ALU.add).then_inc(affine_ready, 1)
                pool.wait_ge(negmr_ready, n + 1)
                pool.tensor_tensor(xbias[b][:, :], negmr[b][:, :], obias[:, :], ALU.add).then_inc(affine_ready, 1)

            for u in range(U):
                image(0, u)
            with pool.Fori(1, STEPS) as s:
                for u in range(U):
                    image(s, u)

        @block.scalar
        def _(act):
            act.wait_ge(w_loaded, 16)
            act.activation(wsign[:, :, :].rearrange("o c t -> o (c t)"), wraw[:, :], ACT.Sign).then_inc(w_signed, 1)
            act.activation(wabs[:, :], wraw[:, :], ACT.Abs, accum_out=wsum[:, :]).then_inc(w_signed, 1)

            def sign(s, u):
                n, b = s * U + u, u % SG
                act.wait_ge(negm_ready, n + 1)
                if u >= SG or not isinstance(s, int):
                    act.wait_ge(conv_done, (n - SG + 1) * CHUNKS)
                act.activation(sg[b][:, :, 1:1 + W], xt[u][:, :].rearrange("c (h w) -> c h w", h=H), ACT.Sign,
                               bias=negm[b][:, 0:1]).then_inc(signed, 1)

            def scale(s, u):
                n, b = s * U + u, u % SG
                act.wait_ge(affine_ready, 2 * (n + 1))
                act.wait_ge(signed, n + 1)
                act.activation(xt[u][:, :], xt[u][:, :], ACT.Identity, bias=xbias[b][:, 0:1],
                               scale=xscale[b][:, 0:1]).then_inc(scaled, 1)

            act.wait_ge(const_ready, 1)
            for u in range(U):
                sign(0, u)
                scale(0, u)
            with act.Fori(1, STEPS) as s:
                for u in range(U):
                    sign(s, u)
                    scale(s, u)

        @block.tensor
        def _(pe):
            pe.wait_ge(ident_ready, 1)
            pe.wait_ge(w_signed, 1)
            turn = [bank[:, 0:O // 2].bitcast(BF16) for bank in conv]
            for t, (ky, kx) in enumerate(taps):
                if t >= CHUNKS:
                    pe.wait_ge(w_ready, t - CHUNKS + 1)
                pe.transpose(turn[t % CHUNKS], wsign[:, :, ky * KW + kx], ident[:, :])\
                    .then_inc(w_turned, 1)
            pe.wait_ge(same_ready, 1)
            pe.wait_ge(w_ready, TAPS)

            def sum_groups(n, b):
                pe.wait_ge(spread_ready, n + 1)
                pe.matmul(small[:, 0:CG * 3], same[:, :, :].rearrange("c g k -> c (g k)"),
                          spread[b][:, :, :].rearrange("c k j -> c (k j)"), start=True, stop=True).then_inc(summed, 1)

            def convolve(n, b, c, first):
                if c == 0:
                    pe.wait_ge(signed, n + 1)
                if not first:
                    pe.wait_ge(chunk_done, (n - 1) * CHUNKS + c + 1)
                for t, (ky, kx) in enumerate(taps):
                    top = max(0, 1 - ky - c * ROWS)
                    end = min(ROWS, H + 1 - ky - c * ROWS)
                    r0 = c * ROWS + top + ky - 1
                    last = pe.matmul(conv[c][:, top * W:end * W], wT[:, t, :],
                                     sg[b][:, r0:r0 + end - top, kx:kx + W], start=(t == 0), stop=(t == TAPS - 1))
                last.then_inc(conv_done, 1)

            def image(s, u, ahead=True):
                for c in range(CHUNKS):
                    convolve(s * U + u, u % SG, c, isinstance(s, int) and s == 0 and u == 0)
                    if c == STATS_AFTER and ahead:
                        sum_groups(s * U + u + 2, u % SG)

            sum_groups(0, 0)
            sum_groups(1, 1)
            for u in range(U):
                image(0, u)
            with pe.Fori(1, STEPS - 1) as s:
                for u in range(U):
                    image(s, u)
            for u in range(U):
                image(STEPS - 1, u, u < U - 2)

        @block.vector
        def _(dve):
            for b in range(SG):
                dve.memset(sg[b][:, :, 0:1], 0.0)
                dve.memset(sg[b][:, :, WP - 1:WP], 0.0)
                dve.memset(chan[b][:, 0:1], 1.0)
            dve.wait_ge(ident_ready, 1)
            dve.tensor_reduce(place[:, :], ident[:, :].rearrange("c (g k) -> c k g", k=CG), AX_X, ALU.add)\
                .then_inc(const_ready, 1)
            dve.wait_ge(const_ready, 1)

            def stats(s, u):
                n, b = s * U + u, u % SG
                dve.wait_ge(x_loaded[u], (s + 1) * 16)
                for c in range(CHUNKS):
                    dve.bn_stats(tuples[b][:, c, :], xt[u][:, c * CHUNK:(c + 1) * CHUNK])
                dve.drain()
                dve.bn_aggr(chan[b][:, 1:3], tuples[b][:, :, :].rearrange("c k j -> c (k j)")).then_inc(chan_ready, 1)
                dve.wait_ge(chan_ready, n + 1)
                dve.tensor_tensor(spread[b][:, :, :], chan[b][:, :].unsqueeze(1).to_broadcast([C, CG, 3]),
                                  place[:, :].unsqueeze(2).to_broadcast([C, CG, 3]), ALU.mult)\
                    .then_inc(spread_ready, 1)

            def groups(s, u):
                n, b = s * U + u, u % SG
                dve.wait_ge(summed, n + 1)
                if u >= SG or not isinstance(s, int):
                    dve.wait_ge(rstd_ready, n - SG + 1)
                dve.tensor_copy(gtuples[:, :], small[:, 0:CG * 3])
                dve.drain()
                dve.bn_aggr(group[b][:, :], gtuples[:, :]).then_inc(group_ready, 1)
                dve.wait_ge(group_ready, n + 1)
                if u >= SG or not isinstance(s, int):
                    dve.wait_ge(negmr_ready, n - SG + 1)
                    dve.wait_ge(signed, n - SG + 1)
                dve.tensor_scalar(negm[b][:, :], group[b][:, 0:1], -1.0, None, ALU.mult).then_inc(negm_ready, 1)

            def finish(s, u, ahead=True):
                n = s * U + u
                for c in range(CHUNKS):
                    if c == 0:
                        dve.wait_ge(scaled, n + 1)
                    dve.wait_ge(conv_done, n * CHUNKS + c + 1)
                    part = xt[u][:, c * CHUNK:(c + 1) * CHUNK]
                    dve.scalar_tensor_tensor(out=part, in0=conv[c][:, 0:CHUNK], scalar=oscale[:, 0:1], in1=part,
                                             op0=ALU.mult, op1=ALU.add).then_inc(chunk_done, 1)
                    if c == STATS_AFTER and ahead:
                        step, tile = (s, u + 2) if u + 2 < U else (s + 1, u + 2 - U)
                        groups(step, tile)

            def ahead_of(s, u):
                return (s, u + 2) if u + 2 < U else (s + 1, u + 2 - U)

            turn = [bank[:, 0:O // 2].bitcast(BF16) for bank in conv]
            for t in range(TAPS):
                dve.wait_ge(w_turned, t + 1)
                dve.tensor_copy(wT[:, t, :], turn[t % CHUNKS]).then_inc(w_ready, 1)
            dve.wait_ge(w_signed, 2)
            dve.tensor_scalar(wmean[:, :], wsum[:, :], 1.0 / (C * TAPS), None, ALU.mult).then_inc(dve_step, 1)
            dve.wait_ge(dve_step, 1)
            dve.wait_ge(bn_ready, 1)
            dve.tensor_tensor(oscale[:, :], wmean[:, :], inv[:, :], ALU.mult).then_inc(oscale_ready, 1)
            dve.wait_ge(oscale_ready, 1)
            stats(0, 0)
            groups(0, 0)
            stats(0, 1)
            groups(0, 1)

            def image(s, u, ahead=True):
                if ahead:
                    stats(*ahead_of(s, u))
                finish(s, u, ahead)

            for u in range(U):
                image(0, u)
            with dve.Fori(1, STEPS - 1) as s:
                for u in range(U):
                    image(s, u)
            for u in range(U):
                image(STEPS - 1, u, u < U - 2)


_INS = ['x', 'L0_conv_weight', 'L0_conv_gamma', 'L0_conv_beta', 'L0_conv_bn_mean', 'L0_conv_bn_var']
_OUTS = [((64, 128, 56, 56), 'float32')]


def kernel(**inputs):
    import numpy as _np
    import concourse.bacc as _bacc
    from concourse import mybir as _mybir
    from concourse.bass_utils import run_bass_kernel_spmd as _run

    nc = _bacc.Bacc("TRN2", target_bir_lowering=False, num_devices=1)
    arrays, args = {}, []
    for name in _INS:
        a = _np.ascontiguousarray(inputs[name])
        arrays[f"in_{name}_dram"] = a
        args.append(nc.dram_tensor(f"in_{name}_dram", a.shape, _mybir.dt.from_np(a.dtype), kind="ExternalInput").ap())
    for i, (shape, dtype) in enumerate(_OUTS):
        dt = _mybir.dt.from_np(_np.dtype(dtype))
        args.append(nc.dram_tensor(f"out_{i}_dram", shape, dt, kind="ExternalOutput").ap())
    gn_binary_conv_kernel(nc, *args)
    r = _run(nc, [arrays], core_ids=[0])
    got = tuple(r.results[0][f"out_{i}_dram"] for i in range(len(_OUTS)))
    return got[0]
```

```python
from contextlib import ExitStack

import concourse.bass as bass
from concourse import mybir

F32 = mybir.dt.float32
F32R = mybir.dt.float32r
BF16 = mybir.dt.bfloat16
FP16 = mybir.dt.float16
I16 = mybir.dt.int16
ALU = mybir.AluOpType
ACT = mybir.ActivationFunctionType
AX_X = mybir.AxisListType.X

GN_EPS = 1e-5
BN_EPS = 1e-5
GROUPS = 32
B = 3072.0


def gn_binary_conv_kernel(nc: bass.Bass, x: bass.AP, weight: bass.AP, gamma: bass.AP, beta: bass.AP,
                          bn_mean: bass.AP, bn_var: bass.AP, out: bass.AP):
    N, C, H, W = x.shape
    O, _, KH, KW = weight.shape
    assert C == 128 and O == 128 and KH == 3 and KW == 3 and H % 8 == 0
    CG = C // GROUPS
    HW = H * W
    TAPS = KH * KW
    TERMS = C * TAPS
    assert 2 * TERMS < B and TERMS * (B + 1) < 2 ** 24
    HH = H // 2
    HALF = HH * W
    CH_ROWS = HH // 4
    CHUNK = CH_ROWS * W
    PARTS = 2
    PART = 2 * CHUNK
    PAIRS = 3
    ST = 7
    PIECE = HW // ST
    WP = W + 2
    U = 6
    SG = 2
    FRONT = 4
    LOOPS = (N - FRONT) // U - 1
    BACK = U * LOOPS + FRONT
    assert HW % ST == 0 and PIECE <= 512 and (PARTS * U) % PAIRS == 0

    x_v = x.rearrange("n c h w -> n c (h w)")
    out_v = out.rearrange("n c h w -> n c (h w)")
    w_v = weight.rearrange("o c kh kw -> o (c kh kw)")
    taps = [(ky, kx) for ky in range(KH) for kx in range(KW)]

    def exists(j, k):
        return not isinstance(j, int) or 0 <= U * j + k < N

    def number(j, k):
        return U * j + k

    def from_image(j, k, first):
        return not isinstance(j, int) or U * j + k >= first

    with ExitStack() as ctx:
        def sb(name, shape, dt=F32):
            return ctx.enter_context(nc.sbuf_tensor(name, shape, dt))

        def psum(name, shape, dt=F32):
            return ctx.enter_context(nc.psum_tensor(name, shape, dt))

        def sem(name):
            return ctx.enter_context(nc.semaphore(name))

        xt = [sb(f"xt{i}", [C, HW]) for i in range(U)]
        sg = [sb(f"sg{i}", [C, H + 2, W], BF16) for i in range(SG)]
        lower = sb("lower", [C, HH + 2, W], BF16)
        pk = [sb(f"pk{i}", [C, HH + 2, WP], F32R) for i in range(SG)]
        bot = [sb(f"bot{i}", [O, HALF], I16) for i in range(SG)]
        botf = [sb(f"botf{i}", [O, HALF], FP16) for i in range(SG)]
        tuples = sb("tuples", [C, ST, 6])
        chan = sb("chan", [C, 3])
        spread = sb("spread", [C, CG, 3])
        gtuples = sb("gtuples", [C, CG * 3])
        group = [sb(f"group{i}", [C, 2]) for i in range(SG)]
        negm = [sb(f"negm{i}", [C, 1]) for i in range(SG)]
        vare = [sb(f"vare{i}", [C, 1]) for i in range(SG)]
        rstd = [sb(f"rstd{i}", [C, 1]) for i in range(SG)]
        xscale = [sb(f"xscale{i}", [C, 1]) for i in range(SG)]
        negmr = [sb(f"negmr{i}", [C, 1]) for i in range(SG)]
        xbias = [sb(f"xbias{i}", [C, 1]) for i in range(SG)]

        ident = sb("ident", [C, C], BF16)
        negb = sb("negb", [C, C], FP16)
        same = sb("same", [C, GROUPS, CG])
        place = sb("place", [C, CG])
        halfneg = sb("halfneg", [C, 1])
        gneps = sb("gneps", [C, 1])
        one = sb("one", [C, 1])
        wraw = sb("wraw", [O, C * TAPS])
        wabs = sb("wabs", [O, C * TAPS])
        wsign = sb("wsign", [O, C, TAPS], BF16)
        wT = sb("wT", [C, TAPS, O], F32R)
        wsum = sb("wsum", [O, 1])
        bn = sb("bn", [O, 4])
        bnvare = sb("bnvare", [O, 1])
        bnr = sb("bnr", [O, 1])
        inv = sb("inv", [O, 1])
        minv = sb("minv", [O, 1])
        obias = sb("obias", [O, 1])
        wmean = sb("wmean", [O, 1])
        oscale = sb("oscale", [O, 1])

        conv = psum("conv", [O, 2 * PAIRS, 512])
        small = psum("small", [C, 512])

        x_loaded = [sem(f"x_loaded{i}") for i in range(U)]
        stored = [sem(f"stored{i}") for i in range(U)]
        w_loaded = sem("w_loaded")
        bn_loaded = sem("bn_loaded")
        pool_step = sem("pool_step")
        ident_ready = sem("ident_ready")
        same_ready = sem("same_ready")
        bn_ready = sem("bn_ready")
        w_signed = sem("w_signed")
        w_turned = sem("w_turned")
        w_ready = sem("w_ready")
        const_ready = sem("const_ready")
        place_ready = sem("place_ready")
        dve_step = sem("dve_step")
        oscale_ready = sem("oscale_ready")
        chan_ready = sem("chan_ready")
        spread_ready = sem("spread_ready")
        summed = sem("summed")
        group_ready = sem("group_ready")
        negm_ready = sem("negm_ready")
        vare_ready = sem("vare_ready")
        rstd_ready = sem("rstd_ready")
        negmr_ready = sem("negmr_ready")
        affine_ready = sem("affine_ready")
        signed = sem("signed")
        scaled = sem("scaled")
        dma_gate = sem("dma_gate")
        pack_gate = sem("pack_gate")
        lower_ready = sem("lower_ready")
        packed = sem("packed")
        sums_done = sem("sums_done")
        bot_ready = sem("bot_ready")
        botf_ready = sem("botf_ready")
        top_ready = sem("top_ready")
        top_done = sem("top_done")
        bot_done = sem("bot_done")

        block = ctx.enter_context(nc.Block())

        def run(engine, step, front):
            for k in range(-front, FRONT):
                step(0, k)
            with engine.Fori(0, LOOPS) as j:
                for k in range(FRONT, FRONT + U):
                    step(j, k)
            for k in range(FRONT, N - U * LOOPS + 1):
                step(LOOPS, k)

        @block.sync
        def _(sp):
            sp.dma_start(wraw[:, :], w_v).then_inc(w_loaded, 16)
            for i, vec in enumerate((gamma, beta, bn_mean, bn_var)):
                sp.dma_start(bn[:, i:i + 1], vec.rearrange("(c a) -> c a", a=1)).then_inc(bn_loaded, 16)

            def load(j, k):
                if from_image(j, k, U):
                    sp.wait_ge(stored[k % U], 16 * (j + k // U))
                    sp.sem_inc(dma_gate, 1)
                sp.dma_start(xt[k % U][:, :], x_v[number(j, k)]).then_inc(x_loaded[k % U], 16)

            def store(j, k):
                n = number(j, k)
                sp.wait_ge(bot_done, n + 1)
                sp.sem_inc(dma_gate, 1)
                sp.wait_ge(top_done, PARTS * (n + 1))
                sp.sem_inc(dma_gate, 1)
                sp.dma_start(out_v[n], xt[k % U][:, :]).then_inc(stored[k % U], 16)

            def step(j, k):
                if exists(j, k):
                    store(j, k)
                if exists(j, k + U - 1):
                    load(j, k + U - 1)

            run(sp, step, U - 1)
            for u in range(U):
                sp.wait_ge(stored[u], 16 * ((N - 1 - u) // U + 1))

        @block.gpsimd
        def _(pool):
            count = [0]

            def chain(ins):
                count[0] += 1
                ins.then_inc(pool_step, 1)
                pool.wait_ge(pool_step, count[0])

            chain(pool.memset(ident[:, :], 0.0))
            pool.affine_select(out=ident[:, :], in_=ident[:, :], compare_op=ALU.not_equal, fill=1.0, base=0,
                               pattern=[[-1, C]], channel_multiplier=1).then_inc(ident_ready, 1)
            chain(pool.memset(same[:, :, :], 1.0))
            chain(pool.affine_select(out=same[:, :, :], in_=same[:, :, :], compare_op=ALU.is_ge, fill=0.0, base=0,
                                     pattern=[[-CG, GROUPS], [0, CG]], channel_multiplier=1))
            pool.affine_select(out=same[:, :, :], in_=same[:, :, :], compare_op=ALU.is_ge, fill=0.0, base=CG - 1,
                               pattern=[[CG, GROUPS], [0, CG]], channel_multiplier=-1).then_inc(same_ready, 1)
            chain(pool.memset(halfneg[:, :], -0.5))
            chain(pool.memset(gneps[:, :], GN_EPS))
            chain(pool.memset(one[:, :], 1.0))
            pool.wait_ge(bn_loaded, 64)
            chain(pool.tensor_scalar(bnvare[:, :], bn[:, 3:4], BN_EPS, None, ALU.add))
            chain(pool.tensor_tensor(bnr[:, :], bnvare[:, :], halfneg[:, :], ALU.pow))
            chain(pool.tensor_tensor(inv[:, :], bnr[:, :], bn[:, 0:1], ALU.mult))
            chain(pool.tensor_tensor(minv[:, :], inv[:, :], bn[:, 2:3], ALU.mult))
            pool.tensor_tensor(obias[:, :], bn[:, 1:2], minv[:, :], ALU.subtract).then_inc(bn_ready, 1)
            pool.wait_ge(bn_ready, 1)
            pool.wait_ge(const_ready, 1)

            def parameters(j, k):
                n, b = number(j, k), k % SG
                pool.wait_ge(group_ready, n + 1)
                pool.tensor_tensor(vare[b][:, :], group[b][:, 1:2], gneps[:, :], ALU.add).then_inc(vare_ready, 1)
                pool.wait_ge(vare_ready, n + 1)
                pool.tensor_tensor(rstd[b][:, :], vare[b][:, :], halfneg[:, :], ALU.pow).then_inc(rstd_ready, 1)
                pool.wait_ge(rstd_ready, n + 1)
                pool.wait_ge(negm_ready, n + 1)
                pool.tensor_tensor(negmr[b][:, :], negm[b][:, :], rstd[b][:, :], ALU.mult).then_inc(negmr_ready, 1)
                if from_image(j, k, SG):
                    pool.wait_ge(scaled, n - SG + 1)
                pool.tensor_tensor(xscale[b][:, :], rstd[b][:, :], one[:, :], ALU.add).then_inc(affine_ready, 1)
                pool.wait_ge(negmr_ready, n + 1)
                pool.tensor_tensor(xbias[b][:, :], negmr[b][:, :], obias[:, :], ALU.add).then_inc(affine_ready, 1)

            def pack(j, k):
                n, b = number(j, k), k % SG
                pool.wait_ge(signed, n + 1)
                if from_image(j, k, 1):
                    pool.wait_ge(packed, n)
                if from_image(j, k, SG):
                    pool.wait_ge(sums_done, PARTS * (n - SG + 1))
                pool.sem_inc(pack_gate, 1)
                pool.tensor_scalar(lower[:, :, :], sg[b][:, HH:H + 2, :], B, 0.0, ALU.mult, ALU.add)\
                    .then_inc(lower_ready, 1)
                pool.wait_ge(lower_ready, n + 1)
                pool.tensor_tensor(pk[b][:, :, 1:1 + W], lower[:, :, :], sg[b][:, 0:HH + 2, :], ALU.add)\
                    .then_inc(packed, 1)

            def step(j, k):
                if exists(j, k + 1):
                    pack(j, k + 1)
                if exists(j, k + 2):
                    parameters(j, k + 2)

            run(pool, step, 2)

        @block.scalar
        def _(act):
            act.wait_ge(w_loaded, 16)
            act.activation(wsign[:, :, :].rearrange("o c t -> o (c t)"), wraw[:, :], ACT.Sign).then_inc(w_signed, 1)
            act.activation(wabs[:, :], wraw[:, :], ACT.Abs, accum_out=wsum[:, :]).then_inc(w_signed, 1)
            act.wait_ge(const_ready, 1)

            def sign(j, k):
                n, b = number(j, k), k % SG
                act.wait_ge(negm_ready, n + 1)
                if from_image(j, k, SG):
                    act.wait_ge(packed, n - SG + 1)
                act.activation(sg[b][:, 1:1 + H, :], xt[k % U][:, :].rearrange("c (h w) -> c h w", h=H), ACT.Sign,
                               bias=negm[b][:, 0:1]).then_inc(signed, 1)

            def scale(j, k):
                n, b = number(j, k), k % SG
                act.wait_ge(affine_ready, 2 * (n + 1))
                act.wait_ge(signed, n + 1)
                act.activation(xt[k % U][:, :], xt[k % U][:, :], ACT.Identity, bias=xbias[b][:, 0:1],
                               scale=xscale[b][:, 0:1]).then_inc(scaled, 1)

            def bottom(j, k, p):
                n, b, pair = number(j, k), k % SG, (PARTS * k + p) % PAIRS
                act.wait_ge(sums_done, PARTS * n + p + 1)
                if from_image(j, k, SG):
                    act.wait_ge(bot_done, n - SG + 1)
                act.activation(bot[b][:, p * PART:(p + 1) * PART].rearrange("o (q m) -> o q m", q=2),
                               conv[:, 2 * pair:2 * pair + 2, 0:CHUNK], ACT.Identity, scale=1.0 / B)\
                    .then_inc(bot_ready, 1)

            def step(j, k):
                if exists(j, k + 1):
                    scale(j, k + 1)
                if exists(j, k):
                    bottom(j, k, 0)
                if exists(j, k + 2):
                    sign(j, k + 2)
                if exists(j, k):
                    bottom(j, k, 1)

            run(act, step, 2)

        @block.tensor
        def _(pe):
            pe.wait_ge(ident_ready, 1)
            pe.wait_ge(w_signed, 1)
            for t in range(TAPS):
                if t >= 2 * PAIRS:
                    pe.wait_ge(w_ready, t - 2 * PAIRS + 1)
                pe.transpose(conv[:, t % (2 * PAIRS), 0:O // 2].bitcast(BF16), wsign[:, :, t], ident[:, :])\
                    .then_inc(w_turned, 1)
            pe.wait_ge(same_ready, 1)
            pe.wait_ge(w_ready, TAPS)
            pe.wait_ge(const_ready, 2)

            def sum_group(j, k):
                pe.wait_ge(spread_ready, number(j, k) + 1)
                pe.matmul(small[:, 0:CG * 3], same[:, :, :].rearrange("c g k -> c (g k)"),
                          spread[:, :, :].rearrange("c k j -> c (k j)"), start=True, stop=True).then_inc(summed, 1)

            def sums(j, k, p, last_chunk=None):
                n, b, pair = number(j, k), k % SG, (PARTS * k + p) % PAIRS
                if p == 0:
                    pe.wait_ge(packed, n + 1)
                if not last_chunk and from_image(j, k, 1 if p else 2):
                    pe.wait_ge(top_done, PARTS * n + p + 1 - PAIRS)
                for q in range(2) if last_chunk is None else (last_chunk,):
                    for t, (ky, kx) in enumerate(taps):
                        r0 = (2 * p + q) * CH_ROWS + ky
                        last = pe.matmul(conv[:, 2 * pair + q, 0:CHUNK], wT[:, t, :],
                                         pk[b][:, r0:r0 + CH_ROWS, kx:kx + W], start=(t == 0), stop=(t == TAPS - 1))
                if last_chunk is not False:
                    last.then_inc(sums_done, 1)

            def take_out(j, k, p):
                n, b, pair = number(j, k), k % SG, (PARTS * k + p) % PAIRS
                pe.wait_ge(botf_ready, PARTS * n + p + 1)
                for q in range(2):
                    c = 2 * p + q
                    last = pe.matmul(conv[:, 2 * pair + q, 0:CHUNK], negb[:, :],
                                     botf[b][:, c * CHUNK:(c + 1) * CHUNK], start=False, stop=True,
                                     skip_group_check=True)
                last.then_inc(top_ready, 1)

            def step(j, k):
                if exists(j, k):
                    sums(j, k, 0)
                if exists(j, k - 1):
                    take_out(j, k - 1, 1)
                if exists(j, k):
                    sums(j, k, 1, False)
                if exists(j, k + 2):
                    sum_group(j, k + 2)
                if exists(j, k):
                    sums(j, k, 1, True)
                    take_out(j, k, 0)

            run(pe, step, 2)

        @block.vector
        def _(dve):
            for b in range(SG):
                dve.memset(sg[b][:, 0:1, :], 0.0)
                dve.memset(sg[b][:, H + 1:H + 2, :], 0.0)
                dve.memset(pk[b][:, :, 0:1].bitcast(F32), 0.0)
                dve.memset(pk[b][:, :, WP - 1:WP].bitcast(F32), 0.0)
            dve.memset(chan[:, 0:1], 1.0).then_inc(const_ready, 1)
            dve.wait_ge(ident_ready, 1)
            dve.tensor_scalar(negb[:, :], ident[:, :], -B, None, ALU.mult).then_inc(const_ready, 1)
            dve.tensor_reduce(place[:, :], ident[:, :].rearrange("c (g k) -> c k g", k=CG), AX_X, ALU.add)\
                .then_inc(place_ready, 1)
            dve.wait_ge(place_ready, 1)
            for t in range(TAPS):
                dve.wait_ge(w_turned, t + 1)
                dve.tensor_copy(wT[:, t, :], conv[:, t % (2 * PAIRS), 0:O // 2].bitcast(BF16)).then_inc(w_ready, 1)
            dve.wait_ge(w_signed, 2)
            dve.tensor_scalar(wmean[:, :], wsum[:, :], 1.0 / TERMS, None, ALU.mult).then_inc(dve_step, 1)
            dve.wait_ge(dve_step, 1)
            dve.wait_ge(bn_ready, 1)
            dve.tensor_tensor(oscale[:, :], wmean[:, :], inv[:, :], ALU.mult).then_inc(oscale_ready, 1)
            dve.wait_ge(oscale_ready, 1)

            def measure(j, k, pieces):
                if 0 in pieces:
                    dve.wait_ge(x_loaded[k % U], 16 * (j + k // U + 1))
                for i in pieces:
                    dve.bn_stats(tuples[:, i, :], xt[k % U][:, i * PIECE:(i + 1) * PIECE])

            def spread_tuple(j, k):
                n = number(j, k)
                dve.drain()
                dve.bn_aggr(chan[:, 1:3], tuples[:, :, :].rearrange("c k j -> c (k j)")).then_inc(chan_ready, 1)
                dve.wait_ge(chan_ready, n + 1)
                if from_image(j, k, 1):
                    dve.wait_ge(summed, n)
                dve.tensor_tensor(spread[:, :, :], chan[:, :].unsqueeze(1).to_broadcast([C, CG, 3]),
                                  place[:, :].unsqueeze(2).to_broadcast([C, CG, 3]), ALU.mult)\
                    .then_inc(spread_ready, 1)

            def group_mean(j, k):
                n, b = number(j, k), k % SG
                if from_image(j, k, SG):
                    dve.wait_ge(negmr_ready, n - SG + 1)
                dve.wait_ge(summed, n + 1)
                dve.tensor_copy(gtuples[:, :], small[:, 0:CG * 3])
                dve.drain()
                dve.bn_aggr(group[b][:, :], gtuples[:, :]).then_inc(group_ready, 1)
                dve.wait_ge(group_ready, n + 1)
                if from_image(j, k, SG):
                    dve.wait_ge(signed, n - SG + 1)
                dve.tensor_scalar(negm[b][:, :], group[b][:, 0:1], -1.0, None, ALU.mult).then_inc(negm_ready, 1)

            def for_tensor(j, k, p):
                n, b = number(j, k), k % SG
                dve.wait_ge(bot_ready, PARTS * n + p + 1)
                if from_image(j, k, SG):
                    dve.wait_ge(top_ready, PARTS * (n - SG) + p + 1)
                dve.tensor_copy(botf[b][:, p * PART:(p + 1) * PART], bot[b][:, p * PART:(p + 1) * PART])\
                    .then_inc(botf_ready, 1)

            def finish_top(j, k, p):
                n, pair = number(j, k), (PARTS * k + p) % PAIRS
                dve.wait_ge(scaled, n + 1)
                dve.wait_ge(top_ready, PARTS * n + p + 1)
                part = xt[k % U][:, p * PART:(p + 1) * PART].rearrange("o (q m) -> o q m", q=2)
                dve.scalar_tensor_tensor(out=part, in0=conv[:, 2 * pair:2 * pair + 2, 0:CHUNK], scalar=oscale[:, 0:1],
                                         in1=part, op0=ALU.mult, op1=ALU.add).then_inc(top_done, 1)

            def finish_bottom(j, k):
                n, b = number(j, k), k % SG
                dve.wait_ge(scaled, n + 1)
                dve.wait_ge(bot_ready, PARTS * (n + 1))
                part = xt[k % U][:, HALF:HW]
                dve.scalar_tensor_tensor(out=part, in0=bot[b][:, :], scalar=oscale[:, 0:1], in1=part,
                                         op0=ALU.mult, op1=ALU.add).then_inc(bot_done, 1)

            def step(j, k):
                if exists(j, k - 1):
                    for_tensor(j, k - 1, 1)
                if exists(j, k + 2):
                    measure(j, k + 2, range(ST))
                    spread_tuple(j, k + 2)
                if exists(j, k):
                    for_tensor(j, k, 0)
                if exists(j, k - 1):
                    finish_top(j, k - 1, 1)
                if exists(j, k + 2):
                    group_mean(j, k + 2)
                if exists(j, k - 1):
                    finish_bottom(j, k - 1)
                if exists(j, k):
                    finish_top(j, k, 0)

            run(dve, step, 2)


_INS = ['x', 'L0_conv_weight', 'L0_conv_gamma', 'L0_conv_beta', 'L0_conv_bn_mean', 'L0_conv_bn_var']
_OUTS = [((64, 128, 56, 56), 'float32')]


def kernel(**inputs):
    import numpy as _np
    import concourse.bacc as _bacc
    from concourse import mybir as _mybir
    from concourse.bass_utils import run_bass_kernel_spmd as _run

    nc = _bacc.Bacc("TRN2", target_bir_lowering=False, num_devices=1)
    arrays, args = {}, []
    for name in _INS:
        a = _np.ascontiguousarray(inputs[name])
        arrays[f"in_{name}_dram"] = a
        args.append(nc.dram_tensor(f"in_{name}_dram", a.shape, _mybir.dt.from_np(a.dtype), kind="ExternalInput").ap())
    for i, (shape, dtype) in enumerate(_OUTS):
        dt = _mybir.dt.from_np(_np.dtype(dtype))
        args.append(nc.dram_tensor(f"out_{i}_dram", shape, dt, kind="ExternalOutput").ap())
    gn_binary_conv_kernel(nc, *args)
    r = _run(nc, [arrays], core_ids=[0])
    got = tuple(r.results[0][f"out_{i}_dram"] for i in range(len(_OUTS)))
    return got[0]
```

```python
from contextlib import ExitStack

import concourse.bass as bass
from concourse import mybir

F32 = mybir.dt.float32
F32R = mybir.dt.float32r
BF16 = mybir.dt.bfloat16
FP16 = mybir.dt.float16
I16 = mybir.dt.int16
ALU = mybir.AluOpType
ACT = mybir.ActivationFunctionType
AX_X = mybir.AxisListType.X

GN_EPS = 1e-5
BN_EPS = 1e-5
GROUPS = 32
B = 3072.0


def gn_binary_conv_kernel(nc: bass.Bass, x: bass.AP, weight: bass.AP, gamma: bass.AP, beta: bass.AP,
                          bn_mean: bass.AP, bn_var: bass.AP, out: bass.AP):
    N, C, H, W = x.shape
    O, _, KH, KW = weight.shape
    assert C == 128 and O == 128 and KH == 3 and KW == 3 and H % 8 == 0
    CG = C // GROUPS
    HW = H * W
    TAPS = KH * KW
    HALF_TAPS = (TAPS + 1) // 2
    TERMS = C * TAPS
    assert 2 * TERMS < B and TERMS * (B + 1) < 2 ** 24
    HH = H // 2
    HALF = HH * W
    CH_ROWS = HH // 4
    CHUNK = CH_ROWS * W
    PARTS = 2
    PART = 2 * CHUNK
    PAIRS = 3
    ST = 7
    PIECE = HW // ST
    WP = W + 2
    TURNS = 4
    U = 12
    SG = 2
    FRONT = 4
    LOOPS = (N - FRONT) // U - 1
    BACK = U * LOOPS + FRONT
    assert HW % ST == 0 and PIECE <= 512 and (PARTS * U) % PAIRS == 0

    x_v = x.rearrange("n c h w -> n c (h w)")
    out_v = out.rearrange("n c h w -> n c (h w)")
    w_v = weight.rearrange("o c kh kw -> o (c kh kw)")
    taps = [(ky, kx) for ky in range(KH) for kx in range(KW)]

    def exists(j, k):
        return not isinstance(j, int) or 0 <= U * j + k < N

    def number(j, k):
        return U * j + k

    def from_image(j, k, first):
        return not isinstance(j, int) or U * j + k >= first

    with ExitStack() as ctx:
        def sb(name, shape, dt=F32):
            return ctx.enter_context(nc.sbuf_tensor(name, shape, dt))

        def psum(name, shape, dt=F32):
            return ctx.enter_context(nc.psum_tensor(name, shape, dt))

        def sem(name):
            return ctx.enter_context(nc.semaphore(name))

        xt = [sb(f"xt{i}", [C, HW]) for i in range(U)]
        sg = [sb(f"sg{i}", [C, H + 2, W], BF16) for i in range(SG)]
        lower = sb("lower", [C, HH + 2, W], BF16)
        pk = [sb(f"pk{i}", [C, HH + 2, WP], F32R) for i in range(SG)]
        bot = [sb(f"bot{i}", [O, HALF], I16) for i in range(SG)]
        botf = [sb(f"botf{i}", [O, HALF], FP16) for i in range(SG)]
        tuples = sb("tuples", [C, ST, 6])
        chan = sb("chan", [C, 3])
        spread = sb("spread", [C, CG, 3])
        group = [sb(f"group{i}", [C, 2]) for i in range(SG)]
        negm = [sb(f"negm{i}", [C, 1]) for i in range(SG)]
        vare = [sb(f"vare{i}", [C, 1]) for i in range(SG)]
        rstd = [sb(f"rstd{i}", [C, 1]) for i in range(SG)]
        xscale = [sb(f"xscale{i}", [C, 1]) for i in range(SG)]
        negmr = [sb(f"negmr{i}", [C, 1]) for i in range(SG)]
        xbias = [sb(f"xbias{i}", [C, 1]) for i in range(SG)]

        ident = sb("ident", [C, C], BF16)
        negb = sb("negb", [C, C], FP16)
        same = sb("same", [C, GROUPS, CG])
        place = sb("place", [C, CG])
        halfneg = sb("halfneg", [C, 1])
        gneps = sb("gneps", [C, 1])
        one = sb("one", [C, 1])
        negone = sb("negone", [C, 1])
        wraw = sb("wraw", [O, C * TAPS])
        wsign = sb("wsign", [O, C, TAPS], BF16)
        wT = sb("wT", [C, TAPS, O], F32R)
        wsum = sb("wsum", [O, 1])
        bn = sb("bn", [O, 4])
        bnvare = sb("bnvare", [O, 1])
        bnr = sb("bnr", [O, 1])
        inv = sb("inv", [O, 1])
        minv = sb("minv", [O, 1])
        obias = sb("obias", [O, 1])
        wmean = sb("wmean", [O, 1])
        oscale = sb("oscale", [O, 1])

        conv = psum("conv", [O, 2 * PAIRS, 512])
        small = psum("small", [C, 512])

        x_loaded = [sem(f"x_loaded{i}") for i in range(U)]
        stored = [sem(f"stored{i}") for i in range(U)]
        w_loaded = sem("w_loaded")
        bn_loaded = sem("bn_loaded")
        pool_step = sem("pool_step")
        ident_ready = sem("ident_ready")
        same_ready = sem("same_ready")
        bn_ready = sem("bn_ready")
        w_signed = sem("w_signed")
        w_turned = sem("w_turned")
        w_ready = sem("w_ready")
        const_ready = sem("const_ready")
        place_ready = sem("place_ready")
        wmean_ready = sem("wmean_ready")
        oscale_ready = sem("oscale_ready")
        chan_ready = sem("chan_ready")
        spread_ready = sem("spread_ready")
        summed = sem("summed")
        group_ready = sem("group_ready")
        negm_ready = sem("negm_ready")
        vare_ready = sem("vare_ready")
        rstd_ready = sem("rstd_ready")
        negmr_ready = sem("negmr_ready")
        affine_ready = sem("affine_ready")
        signed = sem("signed")
        scaled = sem("scaled")
        dma_gate = sem("dma_gate")
        group_gate = sem("group_gate")
        pack_gate = sem("pack_gate")
        lower_ready = sem("lower_ready")
        packed = sem("packed")
        sums_done = sem("sums_done")
        bot_ready = sem("bot_ready")
        botf_ready = sem("botf_ready")
        top_ready = sem("top_ready")
        top_done = sem("top_done")
        bot_done = sem("bot_done")

        block = ctx.enter_context(nc.Block())

        def run(engine, step, front, weights=None):
            for k in range(-front, FRONT):
                step(0, k)
                if k == -front and weights:
                    weights()
            with engine.Fori(0, LOOPS) as j:
                for k in range(FRONT, FRONT + U):
                    step(j, k)
            for k in range(FRONT, N - U * LOOPS + 1):
                step(LOOPS, k)

        @block.sync
        def _(sp):
            def weights():
                sp.dma_start(wraw[:, :], w_v).then_inc(w_loaded, 16)
                for i, vec in enumerate((gamma, beta, bn_mean, bn_var)):
                    sp.dma_start(bn[:, i:i + 1], vec.rearrange("(c a) -> c a", a=1)).then_inc(bn_loaded, 16)

            def load(j, k):
                if from_image(j, k, U):
                    sp.wait_ge(stored[k % U], 16 * (j + k // U))
                    sp.sem_inc(dma_gate, 1)
                sp.dma_start(xt[k % U][:, :], x_v[number(j, k)]).then_inc(x_loaded[k % U], 16)

            def store(j, k):
                n = number(j, k)
                sp.wait_ge(bot_done, n + 1)
                sp.sem_inc(dma_gate, 1)
                sp.wait_ge(top_done, PARTS * (n + 1))
                sp.sem_inc(dma_gate, 1)
                sp.dma_start(out_v[n], xt[k % U][:, :]).then_inc(stored[k % U], 16)

            def step(j, k):
                if exists(j, k):
                    store(j, k)
                if exists(j, k + U - 1):
                    load(j, k + U - 1)

            run(sp, step, U - 1, weights)
            for u in range(U):
                sp.wait_ge(stored[u], 16 * ((N - 1 - u) // U + 1))

        @block.gpsimd
        def _(pool):
            count = [0]

            def chain(ins):
                count[0] += 1
                ins.then_inc(pool_step, 1)
                pool.wait_ge(pool_step, count[0])

            chain(pool.memset(ident[:, :], 0.0))
            pool.affine_select(out=ident[:, :], in_=ident[:, :], compare_op=ALU.not_equal, fill=1.0, base=0,
                               pattern=[[-1, C]], channel_multiplier=1).then_inc(ident_ready, 1)
            chain(pool.memset(same[:, :, :], 1.0))
            chain(pool.affine_select(out=same[:, :, :], in_=same[:, :, :], compare_op=ALU.is_ge, fill=0.0, base=0,
                                     pattern=[[-CG, GROUPS], [0, CG]], channel_multiplier=1))
            pool.affine_select(out=same[:, :, :], in_=same[:, :, :], compare_op=ALU.is_ge, fill=0.0, base=CG - 1,
                               pattern=[[CG, GROUPS], [0, CG]], channel_multiplier=-1).then_inc(same_ready, 1)
            chain(pool.memset(halfneg[:, :], -0.5))
            chain(pool.memset(gneps[:, :], GN_EPS))
            chain(pool.memset(one[:, :], 1.0))
            chain(pool.memset(negone[:, :], -1.0))
            pool.wait_ge(bn_loaded, 64)
            chain(pool.tensor_scalar(bnvare[:, :], bn[:, 3:4], BN_EPS, None, ALU.add))
            chain(pool.tensor_tensor(bnr[:, :], bnvare[:, :], halfneg[:, :], ALU.pow))
            chain(pool.tensor_tensor(inv[:, :], bnr[:, :], bn[:, 0:1], ALU.mult))
            chain(pool.tensor_tensor(minv[:, :], inv[:, :], bn[:, 2:3], ALU.mult))
            pool.tensor_tensor(obias[:, :], bn[:, 1:2], minv[:, :], ALU.subtract).then_inc(bn_ready, 1)
            pool.wait_ge(bn_ready, 1)
            pool.wait_ge(const_ready, 1)

            def parameters(j, k):
                n, b = number(j, k), k % SG
                pool.wait_ge(group_ready, n + 1)
                if from_image(j, k, SG):
                    pool.wait_ge(signed, n - SG + 1)
                pool.tensor_tensor(negm[b][:, :], group[b][:, 0:1], negone[:, :], ALU.mult).then_inc(negm_ready, 1)
                pool.tensor_tensor(vare[b][:, :], group[b][:, 1:2], gneps[:, :], ALU.add).then_inc(vare_ready, 1)
                pool.wait_ge(vare_ready, n + 1)
                pool.tensor_tensor(rstd[b][:, :], vare[b][:, :], halfneg[:, :], ALU.pow).then_inc(rstd_ready, 1)
                pool.wait_ge(rstd_ready, n + 1)
                pool.wait_ge(negm_ready, n + 1)
                pool.tensor_tensor(negmr[b][:, :], negm[b][:, :], rstd[b][:, :], ALU.mult).then_inc(negmr_ready, 1)
                if from_image(j, k, SG):
                    pool.wait_ge(scaled, n - SG + 1)
                pool.tensor_tensor(xscale[b][:, :], rstd[b][:, :], one[:, :], ALU.add).then_inc(affine_ready, 1)
                pool.wait_ge(negmr_ready, n + 1)
                pool.tensor_tensor(xbias[b][:, :], negmr[b][:, :], obias[:, :], ALU.add).then_inc(affine_ready, 1)

            def pack(j, k):
                n, b = number(j, k), k % SG
                pool.wait_ge(signed, n + 1)
                if from_image(j, k, 1):
                    pool.wait_ge(packed, n)
                if from_image(j, k, SG):
                    pool.wait_ge(sums_done, PARTS * (n - SG + 1))
                pool.sem_inc(pack_gate, 1)
                pool.tensor_scalar(lower[:, :, :], sg[b][:, HH:H + 2, :], B, 0.0, ALU.mult, ALU.add)\
                    .then_inc(lower_ready, 1)
                pool.wait_ge(lower_ready, n + 1)
                pool.tensor_tensor(pk[b][:, :, 1:1 + W], lower[:, :, :], sg[b][:, 0:HH + 2, :], ALU.add)\
                    .then_inc(packed, 1)

            def step(j, k):
                if exists(j, k + 1):
                    pack(j, k + 1)
                if exists(j, k + 2):
                    parameters(j, k + 2)

            run(pool, step, 2)

        @block.scalar
        def _(act):
            act.wait_ge(w_loaded, 16)
            act.activation(wsign[:, :, :].rearrange("o c t -> o (c t)"), wraw[:, :], ACT.Sign).then_inc(w_signed, 1)
            act.activation(wraw[:, :], wraw[:, :], ACT.Abs, accum_out=wsum[:, :]).then_inc(w_signed, 1)
            act.wait_ge(const_ready, 1)

            def sign(j, k):
                n, b = number(j, k), k % SG
                act.wait_ge(negm_ready, n + 1)
                if from_image(j, k, SG):
                    act.wait_ge(packed, n - SG + 1)
                act.activation(sg[b][:, 1:1 + H, :], xt[k % U][:, :].rearrange("c (h w) -> c h w", h=H), ACT.Sign,
                               bias=negm[b][:, 0:1]).then_inc(signed, 1)

            def scale(j, k):
                n, b = number(j, k), k % SG
                act.wait_ge(affine_ready, 2 * (n + 1))
                act.wait_ge(signed, n + 1)
                act.activation(xt[k % U][:, :], xt[k % U][:, :], ACT.Identity, bias=xbias[b][:, 0:1],
                               scale=xscale[b][:, 0:1]).then_inc(scaled, 1)

            def bottom(j, k, p):
                n, b, pair = number(j, k), k % SG, (PARTS * k + p) % PAIRS
                act.wait_ge(sums_done, PARTS * n + p + 1)
                if from_image(j, k, SG):
                    act.wait_ge(bot_done, n - SG + 1)
                act.activation(bot[b][:, p * PART:(p + 1) * PART].rearrange("o (q m) -> o q m", q=2),
                               conv[:, 2 * pair:2 * pair + 2, 0:CHUNK], ACT.Copy, scale=1.0 / B)\
                    .then_inc(bot_ready, 1)

            def step(j, k):
                if exists(j, k):
                    bottom(j, k, 0)
                if exists(j, k + 1):
                    scale(j, k + 1)
                if exists(j, k + 2):
                    sign(j, k + 2)
                if exists(j, k):
                    bottom(j, k, 1)

            run(act, step, 2)

        @block.tensor
        def _(pe):
            pe.wait_ge(ident_ready, 1)
            pe.wait_ge(w_signed, 1)
            for t in range(TAPS):
                turned = conv[:, t // TURNS, :].bitcast(BF16)[:, (t % TURNS) * O:(t % TURNS + 1) * O]
                last = pe.transpose(turned, wsign[:, :, t], ident[:, :])
            last.then_inc(w_turned, 1)
            pe.wait_ge(same_ready, 1)
            pe.wait_ge(const_ready, 2)

            def weights():
                pe.wait_ge(w_ready, 1)

            def sum_group(j, k):
                if from_image(j, k, 1):
                    pe.wait_ge(group_ready, number(j, k))
                pe.wait_ge(spread_ready, number(j, k) + 1)
                pe.matmul(small[:, 0:CG * 3], same[:, :, :].rearrange("c g k -> c (g k)"),
                          spread[:, :, :].rearrange("c k j -> c (k j)"), start=True, stop=True).then_inc(summed, 1)

            def sums(j, k, p, some):
                n, b, pair = number(j, k), k % SG, (PARTS * k + p) % PAIRS
                if 0 in some:
                    if p == 0:
                        pe.wait_ge(packed, n + 1)
                    if from_image(j, k, 1 if p else 2):
                        pe.wait_ge(top_done, PARTS * n + p + 1 - PAIRS)
                for t in some:
                    ky, kx = taps[t]
                    for q in range(2):
                        r0 = (2 * p + q) * CH_ROWS + ky
                        last = pe.matmul(conv[:, 2 * pair + q, 0:CHUNK], wT[:, t, :],
                                         pk[b][:, r0:r0 + CH_ROWS, kx:kx + W], start=(t == 0), stop=(t == TAPS - 1))
                if TAPS - 1 in some:
                    last.then_inc(sums_done, 1)

            def take_out(j, k, p):
                n, b, pair = number(j, k), k % SG, (PARTS * k + p) % PAIRS
                pe.wait_ge(botf_ready, PARTS * n + p + 1)
                for q in range(2):
                    c = 2 * p + q
                    last = pe.matmul(conv[:, 2 * pair + q, 0:CHUNK], negb[:, :],
                                     botf[b][:, c * CHUNK:(c + 1) * CHUNK], start=False, stop=True,
                                     skip_group_check=True)
                last.then_inc(top_ready, 1)

            def step(j, k):
                if exists(j, k):
                    sums(j, k, 0, range(TAPS))
                if exists(j, k - 1):
                    take_out(j, k - 1, 1)
                if exists(j, k):
                    sums(j, k, 1, range(0, HALF_TAPS))
                if exists(j, k + 2):
                    sum_group(j, k + 2)
                if exists(j, k):
                    sums(j, k, 1, range(HALF_TAPS, TAPS))
                    take_out(j, k, 0)

            run(pe, step, 2, weights)

        @block.vector
        def _(dve):
            for b in range(SG):
                dve.memset(sg[b][:, 0:1, :], 0.0)
                dve.memset(sg[b][:, H + 1:H + 2, :], 0.0)
                dve.memset(pk[b][:, :, 0:1].bitcast(F32), 0.0)
                dve.memset(pk[b][:, :, WP - 1:WP].bitcast(F32), 0.0)
            dve.memset(chan[:, 0:1], 1.0).then_inc(const_ready, 1)
            dve.wait_ge(ident_ready, 1)
            dve.tensor_scalar(negb[:, :], ident[:, :], -B, None, ALU.mult).then_inc(const_ready, 1)
            dve.tensor_reduce(place[:, :], ident[:, :].rearrange("c (g k) -> c k g", k=CG), AX_X, ALU.add)\
                .then_inc(place_ready, 1)
            dve.wait_ge(place_ready, 1)

            def weights():
                dve.wait_ge(w_turned, 1)
                for t in range(0, TAPS, TURNS):
                    m = min(TURNS, TAPS - t)
                    last = dve.tensor_copy(wT[:, t:t + m, :].rearrange("c t o -> c (t o)"),
                                           conv[:, t // TURNS, :].bitcast(BF16)[:, 0:m * O])
                last.then_inc(w_ready, 1)
                dve.wait_ge(w_signed, 2)
                dve.tensor_scalar(wmean[:, :], wsum[:, :], 1.0 / TERMS, None, ALU.mult).then_inc(wmean_ready, 1)
                dve.wait_ge(wmean_ready, 1)
                dve.wait_ge(bn_ready, 1)
                dve.tensor_tensor(oscale[:, :], wmean[:, :], inv[:, :], ALU.mult).then_inc(oscale_ready, 1)
                dve.wait_ge(oscale_ready, 1)

            def measure(j, k, pieces):
                if 0 in pieces:
                    dve.wait_ge(x_loaded[k % U], 16 * (j + k // U + 1))
                for i in pieces:
                    dve.bn_stats(tuples[:, i, :], xt[k % U][:, i * PIECE:(i + 1) * PIECE])

            def channel_tuple(j, k):
                dve.drain()
                dve.bn_aggr(chan[:, 1:3], tuples[:, :, :].rearrange("c k j -> c (k j)")).then_inc(chan_ready, 1)

            def spread_tuple(j, k):
                n = number(j, k)
                if from_image(j, k, 1):
                    dve.wait_ge(summed, n)
                dve.wait_ge(chan_ready, n + 1)
                dve.tensor_tensor(spread[:, :, :], chan[:, :].unsqueeze(1).to_broadcast([C, CG, 3]),
                                  place[:, :].unsqueeze(2).to_broadcast([C, CG, 3]), ALU.mult)\
                    .then_inc(spread_ready, 1)

            def group_mean(j, k):
                n, b = number(j, k), k % SG
                if from_image(j, k, SG):
                    dve.wait_ge(negmr_ready, n - SG + 1)
                dve.wait_ge(summed, n + 1)
                dve.sem_inc(group_gate, 1)
                dve.bn_aggr(group[b][:, :], small[:, 0:CG * 3]).then_inc(group_ready, 1)

            def for_tensor(j, k, p):
                n, b = number(j, k), k % SG
                dve.wait_ge(bot_ready, PARTS * n + p + 1)
                if from_image(j, k, SG):
                    dve.wait_ge(top_ready, PARTS * (n - SG) + p + 1)
                dve.tensor_copy(botf[b][:, p * PART:(p + 1) * PART], bot[b][:, p * PART:(p + 1) * PART])\
                    .then_inc(botf_ready, 1)

            def finish_top(j, k, p):
                n, pair = number(j, k), (PARTS * k + p) % PAIRS
                dve.wait_ge(scaled, n + 1)
                dve.wait_ge(top_ready, PARTS * n + p + 1)
                part = xt[k % U][:, p * PART:(p + 1) * PART].rearrange("o (q m) -> o q m", q=2)
                dve.scalar_tensor_tensor(out=part, in0=conv[:, 2 * pair:2 * pair + 2, 0:CHUNK], scalar=oscale[:, 0:1],
                                         in1=part, op0=ALU.mult, op1=ALU.add).then_inc(top_done, 1)

            def finish_bottom(j, k):
                n, b = number(j, k), k % SG
                dve.wait_ge(scaled, n + 1)
                dve.wait_ge(bot_ready, PARTS * (n + 1))
                part = xt[k % U][:, HALF:HW]
                dve.scalar_tensor_tensor(out=part, in0=bot[b][:, :], scalar=oscale[:, 0:1], in1=part,
                                         op0=ALU.mult, op1=ALU.add).then_inc(bot_done, 1)

            def step(j, k):
                if exists(j, k + 2):
                    measure(j, k + 2, range(0, 3))
                if exists(j, k - 1):
                    for_tensor(j, k - 1, 1)
                if exists(j, k + 2):
                    measure(j, k + 2, range(3, ST))
                    channel_tuple(j, k + 2)
                if exists(j, k):
                    for_tensor(j, k, 0)
                if exists(j, k + 2):
                    spread_tuple(j, k + 2)
                if exists(j, k - 1):
                    finish_top(j, k - 1, 1)
                if exists(j, k + 2):
                    group_mean(j, k + 2)
                if exists(j, k - 1):
                    finish_bottom(j, k - 1)
                if exists(j, k):
                    finish_top(j, k, 0)

            run(dve, step, 2, weights)


_INS = ['x', 'L0_conv_weight', 'L0_conv_gamma', 'L0_conv_beta', 'L0_conv_bn_mean', 'L0_conv_bn_var']
_OUTS = [((64, 128, 56, 56), 'float32')]


def kernel(**inputs):
    import numpy as _np
    import concourse.bacc as _bacc
    from concourse import mybir as _mybir
    from concourse.bass_utils import run_bass_kernel_spmd as _run

    nc = _bacc.Bacc("TRN2", target_bir_lowering=False, num_devices=1)
    arrays, args = {}, []
    for name in _INS:
        a = _np.ascontiguousarray(inputs[name])
        arrays[f"in_{name}_dram"] = a
        args.append(nc.dram_tensor(f"in_{name}_dram", a.shape, _mybir.dt.from_np(a.dtype), kind="ExternalInput").ap())
    for i, (shape, dtype) in enumerate(_OUTS):
        dt = _mybir.dt.from_np(_np.dtype(dtype))
        args.append(nc.dram_tensor(f"out_{i}_dram", shape, dt, kind="ExternalOutput").ap())
    gn_binary_conv_kernel(nc, *args)
    r = _run(nc, [arrays], core_ids=[0])
    got = tuple(r.results[0][f"out_{i}_dram"] for i in range(len(_OUTS)))
    return got[0]
```
